# Optimizing a Trainium2 kernel written in Bass

```python
import numpy as np
import jax
import jax.numpy as jnp

def _softmax(x, axis=-1):
    return jax.nn.softmax(x, axis=axis)

def _gelu(x):
    return jax.nn.gelu(x, approximate=True)

def _silu(x):
    return jax.nn.silu(x)

def _sigmoid(x):
    return jax.nn.sigmoid(x)

def _layernorm(x, axis=-1, eps=1e-05):
    m = jnp.mean(x, axis=axis, keepdims=True)
    v = jnp.var(x, axis=axis, keepdims=True)
    return (x - m) / jnp.sqrt(v + eps)

def _scatter_add(tgt, idx, src, axis=0):
    return tgt.at[idx].add(src)

def _segment_sum(src, seg, n):
    return jax.ops.segment_sum(src, seg, n)
kernel_name = 'mk_gps_d1_gnn_r8_ed7cc2'

def setup_inputs(seed: int=0):
    np.random.seed(seed)
    _w = jnp.asarray

    def _rec_inputs():
        import jax
        import jax.numpy as jnp
        _gk = jax.random.key(seed)
        x = -0.0003713 + 1 * jax.random.normal(jax.random.fold_in(_gk, 1), (6250, 256), jnp.float32)
        _s = jax.random.randint(jax.random.fold_in(_gk, 2), (50000,), 0, 6250, jnp.int32)
        _d = jax.random.randint(jax.random.fold_in(_gk, 3), (50000,), 0, 6250, jnp.int32)
        _loop = jnp.arange(6250, dtype=jnp.int32)
        src = jnp.concatenate([_s, _d, _loop])
        dst = jnp.concatenate([_d, _s, _loop])
        _o = jnp.argsort(dst, stable=True)
        src = src[_o]
        dst = dst[_o]
        return (x, src, dst)
    x, src, dst = _rec_inputs()

    def _L0_gnn_setup():
        import jax, jax.numpy as jnp
        import numpy as np
        N_NODES = 6250
        N_EDGES = 100000
        F_IN = 256
        F_HID = 128
        F_EMB = 64
        K = 2
        T = 3

        def arma_conv(x, edge_src, edge_dst, init_w, w, root_w, b, num_layers=T):
            n = x.shape[0]
            deg = jax.ops.segment_sum(jnp.ones_like(edge_src, dtype=x.dtype), edge_dst, num_segments=n)
            dinv = jnp.where(deg > 0, deg ** (-0.5), 0.0)
            norm = dinv[edge_src] * dinv[edge_dst]
            root = jnp.einsum('nf,kfg->nkg', x, root_w)
            out = None
            for t in range(num_layers):
                if t == 0:
                    h = jnp.einsum('nf,kfg->nkg', x, init_w)
                else:
                    h = jnp.einsum('nkf,kfg->nkg', out, w)
                msg = h[edge_src] * norm[:, None, None]
                h = jax.ops.segment_sum(msg, edge_dst, num_segments=n)
                h = h + root + b[None]
                out = jax.nn.relu(h)
            return out.mean(axis=1)
        key = jax.random.key(seed)
        ks = jax.random.split(key, 16)
        s = 0.05
        x = jax.random.normal(ks[0], (N_NODES, F_IN), dtype=jnp.float32)
        edge_index = jax.random.randint(ks[1], (2, N_EDGES), 0, N_NODES, dtype=jnp.int64)
        return {'x': x, 'edge_index': edge_index, 'init_w1': jax.random.normal(ks[2], (K, F_IN, F_HID), jnp.float32) * s, 'w1': jax.random.normal(ks[3], (K, F_HID, F_HID), jnp.float32) * s, 'root_w1': jax.random.normal(ks[4], (K, F_IN, F_HID), jnp.float32) * s, 'b1': jnp.zeros((K, F_HID), jnp.float32), 'init_w2': jax.random.normal(ks[5], (K, F_HID, F_EMB), jnp.float32) * s, 'w2': jax.random.normal(ks[6], (K, F_EMB, F_EMB), jnp.float32) * s, 'root_w2': jax.random.normal(ks[7], (K, F_HID, F_EMB), jnp.float32) * s, 'b2': jnp.zeros((K, F_EMB), jnp.float32), 'fc1_w': jax.random.normal(ks[8], (F_EMB, F_HID), jnp.float32) * s, 'fc1_b': jnp.zeros((F_HID,), jnp.float32), 'fc2_w': jax.random.normal(ks[9], (F_HID, F_IN), jnp.float32) * s, 'fc2_b': jnp.zeros((F_IN,), jnp.float32)}
    _L0_gnn_all = _L0_gnn_setup()
    _L0_gnn_in = {k: v for k, v in _L0_gnn_all.items() if k in ('init_w1', 'w1', 'root_w1', 'b1', 'init_w2', 'w2', 'root_w2', 'b2', 'fc1_w', 'fc1_b', 'fc2_w', 'fc2_b')}
    del _L0_gnn_all

    def _L0_mix_setup():
        import jax, jax.numpy as jnp
        import numpy as np
        import math
        EMBED = 256
        HEADS = 4
        HEAD_DIM = EMBED // HEADS
        OUT_DIM = 256
        LN_EPS = 1e-05

        def _qkv_init(key):
            spread = math.sqrt(3.0 / EMBED)
            gain, delta = (0.01, 0.01)
            w = jax.random.uniform(key, (EMBED, EMBED), minval=-spread, maxval=spread) * gain
            return w + delta * jnp.eye(EMBED, dtype=w.dtype)

        def _layer_norm(x, g, b):
            mu = jnp.mean(x, axis=-1, keepdims=True)
            var = jnp.mean(jnp.square(x - mu), axis=-1, keepdims=True)
            return (x - mu) * jax.lax.rsqrt(var + LN_EPS) * g + b

        def _split_heads(x, B, S):
            return x.reshape(B, S, HEADS, HEAD_DIM).transpose(0, 2, 1, 3)
        key = jax.random.key(seed)
        ks = jax.random.split(key, 6)
        seq = jax.random.normal(ks[0], (4, 1024, EMBED), dtype=jnp.float32)
        wq = _qkv_init(ks[1])
        wk = _qkv_init(ks[2])
        wv = _qkv_init(ks[3])
        bound = 1.0 / math.sqrt(EMBED)
        wo = jax.random.uniform(ks[4], (OUT_DIM, EMBED), minval=-bound, maxval=bound)
        bo = jax.random.uniform(ks[5], (OUT_DIM,), minval=-bound, maxval=bound)
        ln_k_g = jnp.ones((HEAD_DIM,), jnp.float32)
        ln_k_b = jnp.zeros((HEAD_DIM,), jnp.float32)
        ln_v_g = jnp.ones((HEAD_DIM,), jnp.float32)
        ln_v_b = jnp.zeros((HEAD_DIM,), jnp.float32)
        return {'seq': seq, 'wq': wq, 'wk': wk, 'wv': wv, 'wo': wo, 'bo': bo, 'ln_k_g': ln_k_g, 'ln_k_b': ln_k_b, 'ln_v_g': ln_v_g, 'ln_v_b': ln_v_b}
    _L0_mix_all = _L0_mix_setup()
    _L0_mix_in = {k: v for k, v in _L0_mix_all.items() if k in ('wq', 'wk', 'wv', 'wo', 'bo', 'ln_k_g', 'ln_k_b', 'ln_v_g', 'ln_v_b')}
    del _L0_mix_all

    def _L0_ffn_setup():
        import jax, jax.numpy as jnp
        import numpy as np
        E, D, H, TOP_K = (6, 256, 256, 2)
        ROUTER_H = D // 2
        key = jax.random.key(seed)
        ks = jax.random.split(key, 12)
        s = 1.0 / np.sqrt(D)
        sh = 1.0 / np.sqrt(H)
        sr = 1.0 / np.sqrt(ROUTER_H)
        return {'features': jax.random.normal(ks[0], (8, 512, D), dtype=jnp.float32), 'router_w1': jax.random.uniform(ks[1], (D, ROUTER_H), jnp.float32, -s, s), 'router_b1': jnp.zeros((ROUTER_H,), jnp.float32), 'router_w2': jax.random.uniform(ks[2], (ROUTER_H, E), jnp.float32, -sr, sr), 'router_b2': jnp.zeros((E,), jnp.float32), 'expert_w1': jax.random.uniform(ks[3], (E, D, H), jnp.float32, -s, s), 'expert_b1': jnp.zeros((E, H), jnp.float32), 'expert_w2': jax.random.uniform(ks[4], (E, H, H), jnp.float32, -sh, sh), 'expert_b2': jnp.zeros((E, H), jnp.float32), 'expert_w3': jax.random.uniform(ks[5], (E, H, D), jnp.float32, -sh, sh), 'expert_b3': jnp.zeros((E, D), jnp.float32)}
    _L0_ffn_all = _L0_ffn_setup()
    _L0_ffn_in = {k: v for k, v in _L0_ffn_all.items() if k in ('router_w1', 'router_b1', 'router_w2', 'router_b2', 'expert_w1', 'expert_b1', 'expert_w2', 'expert_b2', 'expert_w3', 'expert_b3')}
    del _L0_ffn_all
    return {'x': x, 'src': src, 'dst': dst, 'L0_gnn_init_w1': _L0_gnn_in['init_w1'], 'L0_gnn_w1': _L0_gnn_in['w1'], 'L0_gnn_root_w1': _L0_gnn_in['root_w1'], 'L0_gnn_b1': _L0_gnn_in['b1'], 'L0_gnn_init_w2': _L0_gnn_in['init_w2'], 'L0_gnn_w2': _L0_gnn_in['w2'], 'L0_gnn_root_w2': _L0_gnn_in['root_w2'], 'L0_gnn_b2': _L0_gnn_in['b2'], 'L0_gnn_fc1_w': _L0_gnn_in['fc1_w'], 'L0_gnn_fc1_b': _L0_gnn_in['fc1_b'], 'L0_gnn_fc2_w': _L0_gnn_in['fc2_w'], 'L0_gnn_fc2_b': _L0_gnn_in['fc2_b'], 'L0_mix_wq': _L0_mix_in['wq'], 'L0_mix_wk': _L0_mix_in['wk'], 'L0_mix_wv': _L0_mix_in['wv'], 'L0_mix_wo': _L0_mix_in['wo'], 'L0_mix_bo': _L0_mix_in['bo'], 'L0_mix_ln_k_g': _L0_mix_in['ln_k_g'], 'L0_mix_ln_k_b': _L0_mix_in['ln_k_b'], 'L0_mix_ln_v_g': _L0_mix_in['ln_v_g'], 'L0_mix_ln_v_b': _L0_mix_in['ln_v_b'], 'L0_ffn_router_w1': _L0_ffn_in['router_w1'], 'L0_ffn_router_b1': _L0_ffn_in['router_b1'], 'L0_ffn_router_w2': _L0_ffn_in['router_w2'], 'L0_ffn_router_b2': _L0_ffn_in['router_b2'], 'L0_ffn_expert_w1': _L0_ffn_in['expert_w1'], 'L0_ffn_expert_b1': _L0_ffn_in['expert_b1'], 'L0_ffn_expert_w2': _L0_ffn_in['expert_w2'], 'L0_ffn_expert_b2': _L0_ffn_in['expert_b2'], 'L0_ffn_expert_w3': _L0_ffn_in['expert_w3'], 'L0_ffn_expert_b3': _L0_ffn_in['expert_b3']}

def reference(x, src, dst, L0_gnn_init_w1, L0_gnn_w1, L0_gnn_root_w1, L0_gnn_b1, L0_gnn_init_w2, L0_gnn_w2, L0_gnn_root_w2, L0_gnn_b2, L0_gnn_fc1_w, L0_gnn_fc1_b, L0_gnn_fc2_w, L0_gnn_fc2_b, L0_mix_wq, L0_mix_wk, L0_mix_wv, L0_mix_wo, L0_mix_bo, L0_mix_ln_k_g, L0_mix_ln_k_b, L0_mix_ln_v_g, L0_mix_ln_v_b, L0_ffn_router_w1, L0_ffn_router_b1, L0_ffn_router_w2, L0_ffn_router_b2, L0_ffn_expert_w1, L0_ffn_expert_b1, L0_ffn_expert_w2, L0_ffn_expert_b2, L0_ffn_expert_w3, L0_ffn_expert_b3):
    import jax
    import jax.numpy as jnp

    def _L0_gnn_ref(x, edge_index, init_w1, w1, root_w1, b1, init_w2, w2, root_w2, b2, fc1_w, fc1_b, fc2_w, fc2_b):
        import jax, jax.numpy as jnp
        import numpy as np
        N_NODES = 6250
        N_EDGES = 100000
        F_IN = 256
        F_HID = 128
        F_EMB = 64
        K = 2
        T = 3

        def arma_conv(x, edge_src, edge_dst, init_w, w, root_w, b, num_layers=T):
            n = x.shape[0]
            deg = jax.ops.segment_sum(jnp.ones_like(edge_src, dtype=x.dtype), edge_dst, num_segments=n)
            dinv = jnp.where(deg > 0, deg ** (-0.5), 0.0)
            norm = dinv[edge_src] * dinv[edge_dst]
            root = jnp.einsum('nf,kfg->nkg', x, root_w)
            out = None
            for t in range(num_layers):
                if t == 0:
                    h = jnp.einsum('nf,kfg->nkg', x, init_w)
                else:
                    h = jnp.einsum('nkf,kfg->nkg', out, w)
                msg = h[edge_src] * norm[:, None, None]
                h = jax.ops.segment_sum(msg, edge_dst, num_segments=n)
                h = h + root + b[None]
                out = jax.nn.relu(h)
            return out.mean(axis=1)
        src, dst = (edge_index[0], edge_index[1])
        h = jax.nn.relu(arma_conv(x, src, dst, init_w1, w1, root_w1, b1))
        latent = jax.nn.relu(arma_conv(h, src, dst, init_w2, w2, root_w2, b2))
        d = jax.nn.relu(latent @ fc1_w + fc1_b)
        reconstructed = d @ fc2_w + fc2_b
        return reconstructed

    def _L0_mix_ref(seq, wq, wk, wv, wo, bo, ln_k_g, ln_k_b, ln_v_g, ln_v_b):
        import jax, jax.numpy as jnp
        import numpy as np
        import math
        EMBED = 256
        HEADS = 4
        HEAD_DIM = EMBED // HEADS
        OUT_DIM = 256
        LN_EPS = 1e-05

        def _qkv_init(key):
            spread = math.sqrt(3.0 / EMBED)
            gain, delta = (0.01, 0.01)
            w = jax.random.uniform(key, (EMBED, EMBED), minval=-spread, maxval=spread) * gain
            return w + delta * jnp.eye(EMBED, dtype=w.dtype)

        def _layer_norm(x, g, b):
            mu = jnp.mean(x, axis=-1, keepdims=True)
            var = jnp.mean(jnp.square(x - mu), axis=-1, keepdims=True)
            return (x - mu) * jax.lax.rsqrt(var + LN_EPS) * g + b

        def _split_heads(x, B, S):
            return x.reshape(B, S, HEADS, HEAD_DIM).transpose(0, 2, 1, 3)
        B, S, _ = seq.shape
        q = _split_heads(seq @ wq.T, B, S)
        k = _split_heads(seq @ wk.T, B, S)
        v = _split_heads(seq @ wv.T, B, S)
        k = _layer_norm(k, ln_k_g, ln_k_b)
        v = _layer_norm(v, ln_v_g, ln_v_b)
        kv = jnp.einsum('bhsd,bhse->bhde', k, v) / S
        ga = jnp.einsum('bhsd,bhde->bhse', q, kv)
        ga = ga.transpose(0, 2, 1, 3).reshape(B, S, EMBED)
        return ga @ wo.T + bo

    def _L0_ffn_ref(features, router_w1, router_b1, router_w2, router_b2, expert_w1, expert_b1, expert_w2, expert_b2, expert_w3, expert_b3):
        import jax, jax.numpy as jnp
        import numpy as np
        E, D, H, TOP_K = (6, 256, 256, 2)
        ROUTER_H = D // 2
        rh = jax.nn.relu(features @ router_w1 + router_b1)
        expert_logits = jax.nn.softmax(rh @ router_w2 + router_b2, axis=-1)
        top_w, top_i = jax.lax.top_k(expert_logits, TOP_K)
        routing_weights = jax.nn.softmax(top_w, axis=-1)
        h1 = jax.nn.relu(jnp.einsum('bsd,edh->bseh', features, expert_w1) + expert_b1)
        h2 = jax.nn.relu(jnp.einsum('bseh,ehf->bsef', h1, expert_w2) + expert_b2)
        expert_out = jnp.einsum('bsef,efo->bseo', h2, expert_w3) + expert_b3
        sel = jnp.take_along_axis(expert_out, top_i[:, :, :, None], axis=2)
        combined = jnp.sum(sel * routing_weights[..., None], axis=2)
        return combined
    edge_index = jnp.stack([src, dst])
    xn = _layernorm(x, axis=-1)
    x = x + _L0_gnn_ref(xn, edge_index, L0_gnn_init_w1, L0_gnn_w1, L0_gnn_root_w1, L0_gnn_b1, L0_gnn_init_w2, L0_gnn_w2, L0_gnn_root_w2, L0_gnn_b2, L0_gnn_fc1_w, L0_gnn_fc1_b, L0_gnn_fc2_w, L0_gnn_fc2_b) + _L0_mix_ref(xn[None], L0_mix_wq, L0_mix_wk, L0_mix_wv, L0_mix_wo, L0_mix_bo, L0_mix_ln_k_g, L0_mix_ln_k_b, L0_mix_ln_v_g, L0_mix_ln_v_b)[0]
    x = x + _L0_ffn_ref(_layernorm(x, axis=-1)[None], L0_ffn_router_w1, L0_ffn_router_b1, L0_ffn_router_w2, L0_ffn_router_b2, L0_ffn_expert_w1, L0_ffn_expert_b1, L0_ffn_expert_w2, L0_ffn_expert_b2, L0_ffn_expert_w3, L0_ffn_expert_b3)[0]
    return x

_drawn_inputs = setup_inputs


def setup_inputs(seed=0):
    import zlib

    import numpy as np

    out = dict(_drawn_inputs(seed))
    spreads = {'L0_gnn_b1': (0.0, 0.8),
     'L0_gnn_b2': (0.0, 2.0),
     'L0_gnn_fc1_b': (0.0, 0.8),
     'L0_gnn_fc2_b': (0.0, 0.514),
     'L0_mix_ln_k_g': (1.0, 0.6),
     'L0_mix_ln_k_b': (0.0, 0.8),
     'L0_mix_ln_v_g': (1.0, 0.6),
     'L0_mix_ln_v_b': (0.0, 0.8),
     'L0_ffn_router_b1': (0.0, 0.8),
     'L0_ffn_router_b2': (0.0, 0.725),
     'L0_ffn_expert_b1': (0.0, 2.0),
     'L0_ffn_expert_b2': (0.0, 1.894),
     'L0_ffn_expert_b3': (0.0, 0.717)}
    factors = {'L0_gnn_init_w1': 21.688,
     'L0_gnn_w1': 6.979,
     'L0_gnn_root_w1': 2.989,
     'L0_gnn_init_w2': 8.0,
     'L0_gnn_w2': 5.109,
     'L0_mix_wq': 6.636,
     'L0_mix_wk': 6.67,
     'L0_mix_wv': 7.119,
     'L0_mix_wo': 6.438,
     'L0_mix_bo': 8.0,
     'L0_ffn_router_w1': 3.473,
     'L0_ffn_router_w2': 3.181,
     'L0_ffn_expert_w1': 5.872,
     'L0_ffn_expert_w2': 4.333,
     'L0_ffn_expert_w3': 2.982}
    for name, (base, spread) in spreads.items():
        noise = np.random.default_rng([zlib.crc32(name.encode()), seed]).standard_normal(out[name].shape)
        drawn = base * np.exp(spread * noise) if base else spread * noise
        out[name] = jnp.asarray(drawn.astype(out[name].dtype))
    for name, factor in factors.items():
        out[name] = (out[name] * factor).astype(out[name].dtype)
    return out
```

```python
from contextlib import ExitStack

import concourse.bass as bass
from concourse import mybir

ALU = mybir.AluOpType
ACT = mybir.ActivationFunctionType
X = mybir.AxisListType.X
F32 = mybir.dt.float32
F16 = mybir.dt.float16
I32 = mybir.dt.int32
DVE = mybir.EngineType.DVE
PE = mybir.EngineType.PE

P = 128
N = 6250
E = 106250
D = 256
TILES = -(-N // P)
NP = TILES * P
LAST = N - (TILES - 1) * P
WIN = 448
WINS = NP // WIN
G = 8
COLS = G * TILES
GPI = 8
TURNS = WIN // G // GPI
GROUPS = NP // G
SUB = 7
CHUNKS = P * SUB
ROW = SUB * P
FULL = E // ROW
EMPTY = -(-E // P) + 1
BATCHES = TILES // SUB
NOWHERE = 8191
PIECES = 7
PT = TILES // PIECES
EPS = 1e-5
EXPERTS = 6


class Steps:

    def __init__(self, eng, sem, base=0):
        self.eng, self.sem, self.base, self.n = eng, sem, base, 0

    def done(self, ins):
        ins.then_inc(self.sem, 1)
        self.n += 1

    def settle(self):
        self.eng.wait_ge(self.sem, self.base + self.n)

    def then(self, ins):
        self.done(ins)
        self.settle()


def gps_layer(nc, a, out):

    def dram(name, shape, dt):
        return nc.dram_tensor(name, shape, dt, kind="Internal").ap()

    adj_d = dram("adj_d", (WINS, P, TILES * WIN), F16)
    chunk_lo_d = dram("chunk_lo_d", (P, SUB), F32)
    chunk_hi_d = dram("chunk_hi_d", (P, SUB), F32)
    bounds_d = dram("bounds_d", (P, SUB * 2), I32)
    dinv_d = dram("dinv_d", (TILES, P), F32)
    xnT_d = dram("xnT_d", (P, 2 * NP), F32)
    root1_d = dram("root1_d", (P, 2 * NP), F32)

    with ExitStack() as whole:
        def sem(name):
            return whole.enter_context(nc.semaphore(name))

        def keep(name, shape, dt):
            return whole.enter_context(nc.sbuf_tensor(name, shape, dt))

        ident = keep("ident", [P, P], F32)
        dinv = keep("dinv", [P, TILES], F32)

        edges = ExitStack()
        key_col = edges.enter_context(nc.sbuf_tensor("key_col", [P, CHUNKS], F32))
        lane_col = edges.enter_context(nc.sbuf_tensor("lane_col", [P, CHUNKS], F32))
        bounds = edges.enter_context(nc.sbuf_tensor("bounds", [1, GROUPS * 2], I32))
        with ExitStack() as ph:
            def sb(name, shape, dt):
                return ph.enter_context(nc.sbuf_tensor(name, shape, dt))

            src_i = sb("src_i", [P, ROW], I32)
            dst_i = sb("dst_i", [P, ROW], I32)
            lane_i = sb("lane_i", [P, ROW], I32)
            tile_i = sb("tile_i", [P, ROW], I32)
            dst_f = sb("dst_f", [P, ROW], F32)
            lane_f = sb("lane_f", [P, ROW], F32)
            tile_f = sb("tile_f", [P, ROW], F32)
            key_f = sb("key_f", [P, ROW], F32)
            low = sb("low", [P, SUB], F32)
            high = sb("high", [P, SUB], F32)
            low_b = sb("low_b", [P, CHUNKS], F32)
            high_b = sb("high_b", [P, CHUNKS], F32)
            from_end = sb("from_end", [P, CHUNKS], F32)
            from_start = sb("from_start", [P, CHUNKS], F32)
            g_first = sb("g_first", [P, SUB], F32)
            g_last = sb("g_last", [P, SUB], F32)
            touch = sb("touch", [P, CHUNKS], F32)
            junk = sb("junk", [P, CHUNKS], F32)
            first = sb("first", [P, SUB], F32)
            last = sb("last", [P, SUB], F32)
            bounds_f = sb("bounds_f", [P, SUB, 2], F32)
            bounds_i = sb("bounds_i", [P, SUB * 2], I32)
            turned = [ph.enter_context(nc.psum_tensor(f"turned{i}", [P, 4, P], F32)) for i in range(4)]

            e_pad, e_in, e_tab, e_turn, e_low, e_lowd, e_lowb, e_bnd, e_bndd, e_bndb, e_const, e_v = (
                sem(n) for n in ("e_padded", "e_loaded", "e_tables", "e_turned", "e_low", "e_low_stored",
                                 "e_low_back", "e_bounds", "e_bounds_stored", "e_bounds_back", "e_const", "e_steps"))
            with nc.Block() as block:
                @block.sync
                def _(sp):
                    sp.wait_ge(e_pad, 2)
                    for rows, flat in ((src_i, a["src"]), (dst_i, a["dst"])):
                        sp.dma_start(rows[0:FULL, :], flat[0:FULL * ROW].rearrange("(p x) -> p x", x=ROW)).then_inc(e_in, 16)
                        sp.dma_start(rows[FULL:FULL + 1, 0:E - FULL * ROW],
                                     flat[FULL * ROW:E].rearrange("(p x) -> p x", p=1)).then_inc(e_in, 16)
                    sp.wait_ge(e_low, 2)
                    sp.dma_start(chunk_lo_d[:, :], low[:, :]).then_inc(e_lowd, 16)
                    sp.dma_start(chunk_hi_d[:, :], high[:, :]).then_inc(e_lowd, 16)
                    sp.wait_ge(e_lowd, 32)
                    for to, of in ((low_b, chunk_lo_d), (high_b, chunk_hi_d)):
                        row = of.rearrange("p (o j) -> o (p j)", o=1)
                        sp.dma_start(to[:, :], row.broadcast_to([P, CHUNKS])).then_inc(e_lowb, 16)
                    sp.wait_ge(e_bnd, 1)
                    sp.dma_start(bounds_d[:, :], bounds_i[:, :]).then_inc(e_bndd, 16)
                    sp.wait_ge(e_bndd, 16)
                    sp.dma_start(bounds[:, :], bounds_d.rearrange("p (o j) -> o (p j)", o=1)[:, 0:GROUPS * 2]).then_inc(e_bndb, 16)
                    sp.wait_ge(e_bndb, 16)

                @block.gpsimd
                def _(pool):
                    nc.gpsimd.iota(g_first[:, :], [[G, SUB]], base=0, channel_multiplier=G * SUB, allow_small_or_imprecise_dtypes=True).then_inc(e_const, 1)
                    nc.gpsimd.iota(g_last[:, :], [[G, SUB]], base=G - 1, channel_multiplier=G * SUB, allow_small_or_imprecise_dtypes=True).then_inc(e_const, 1)
                    nc.gpsimd.iota(from_end[:, :], [[-1, CHUNKS]], base=EMPTY, channel_multiplier=0, allow_small_or_imprecise_dtypes=True).then_inc(e_const, 1)
                    nc.gpsimd.iota(from_start[:, :], [[1, CHUNKS]], base=1, channel_multiplier=0, allow_small_or_imprecise_dtypes=True).then_inc(e_const, 1)
                    nc.gpsimd.memset(ident[:, :], 0.0).then_inc(e_const, 1)
                    pool.wait_ge(e_const, 5)
                    nc.gpsimd.affine_select(out=ident[:, :], in_=ident[:, :], compare_op=ALU.not_equal, fill=1.0, base=0,
                                            pattern=[[-1, P]], channel_multiplier=1).then_inc(e_const, 1)

                @block.vector
                def _(dve):
                    v = Steps(dve, e_v)
                    nc.vector.memset(src_i[:, :], 0).then_inc(e_pad, 1)
                    nc.vector.memset(dst_i[:, :], NOWHERE).then_inc(e_pad, 1)
                    dve.wait_ge(e_in, 64)
                    v.done(nc.vector.tensor_scalar(lane_i[:, :], src_i[:, :], P - 1, None, ALU.bitwise_and))
                    v.done(nc.vector.tensor_scalar(tile_i[:, :], src_i[:, :], 7, None, ALU.logical_shift_right))
                    v.then(nc.vector.tensor_copy(dst_f[:, :], dst_i[:, :]))
                    nc.vector.tensor_reduce(low[:, :], dst_f[:, :].rearrange("p (j e) -> p j e", j=SUB), X, ALU.min).then_inc(e_low, 1)
                    nc.vector.tensor_reduce(high[:, :], dst_f[:, :].rearrange("p (j e) -> p j e", j=SUB), X, ALU.max).then_inc(e_low, 1)
                    nc.vector.tensor_copy(lane_f[:, :], lane_i[:, :]).then_inc(e_tab, 1)
                    v.then(nc.vector.tensor_copy(tile_f[:, :], tile_i[:, :]))
                    nc.vector.scalar_tensor_tensor(key_f[:, :], dst_f[:, :], float(TILES), tile_f[:, :], ALU.mult, ALU.add).then_inc(e_tab, 1)
                    for i, (col, at) in enumerate(((key_col, 0), (key_col, 4), (lane_col, 0), (lane_col, 4))):
                        w = min(4, SUB - at)
                        dve.wait_ge(e_turn, i + 1)
                        to = col[:, :].rearrange("e (p j) -> e j p", j=SUB)[:, at:at + w, :]
                        v.done(nc.vector.tensor_copy(to, turned[i][:, 0:w, :]))
                    dve.wait_ge(e_lowb, 32)
                    dve.wait_ge(e_const, 4)
                    for q in range(SUB):
                        v.then(nc.vector.tensor_scalar(touch[:, :], low_b[:, :], g_last[:, q:q + 1], None, ALU.is_le))
                        v.then(nc.vector.scalar_tensor_tensor(touch[:, :], high_b[:, :], g_first[:, q:q + 1], touch[:, :], ALU.is_ge, ALU.mult))
                        v.then(nc.vector.tensor_tensor_reduce(junk[:, :], touch[:, :], from_end[:, :], 1.0, 0.0, ALU.mult, ALU.max, first[:, q:q + 1]))
                        v.then(nc.vector.tensor_tensor_reduce(junk[:, :], touch[:, :], from_start[:, :], 1.0, 0.0, ALU.mult, ALU.max, last[:, q:q + 1]))
                    v.done(nc.vector.tensor_scalar(bounds_f[:, :, 0], first[:, :], -1.0, float(EMPTY), ALU.mult, ALU.add))
                    v.then(nc.vector.tensor_copy(bounds_f[:, :, 1], last[:, :]))
                    nc.vector.tensor_copy(bounds_i[:, :], bounds_f[:, :, :].rearrange("p j b -> p (j b)")).then_inc(e_bnd, 1)
                    v.settle()

                @block.tensor
                def _(pe):
                    pe.wait_ge(e_const, 6)
                    pe.wait_ge(e_tab, 2)
                    for i, (rows, at) in enumerate(((key_f, 0), (key_f, 4), (lane_f, 0), (lane_f, 4))):
                        for j in range(at, min(at + 4, SUB)):
                            t = nc.tensor.transpose(turned[i][:, j - at, :], rows[:, j * P:(j + 1) * P], ident[:, :])
                        t.then_inc(e_turn, 1)

        with ExitStack() as ph:
            def sb(name, shape, dt):
                return ph.enter_context(nc.sbuf_tensor(name, shape, dt))

            RING = 8
            BANKS = 4
            iota_f = sb("iota_f", [P, COLS], F32)
            iota_col = sb("iota_col", [P, COLS], F16)
            iota_lane = sb("iota_lane", [P, P], F16)
            g_base = sb("g_base", [P, GROUPS], F32)
            place = sb("place", [P, RING, COLS], F16)
            lane = sb("lane", [P, RING, P], F16)
            place_x = sb("place_x", [P, COLS], F16)
            lane_x = sb("lane_x", [P, P], F16)
            stage = sb("stage", [P, 2, TILES, WIN], F16)
            ones16 = sb("ones16", [P, 1], F16)
            zero16 = sb("zero16", [P, WIN], F16)
            one32 = sb("one32", [1, 1], F32)
            deg_row = sb("deg_row", [1, (WINS + 1) * WIN], F32)
            group_ps = [ph.enter_context(nc.psum_tensor(f"group_ps{i}", [P, COLS], F32)) for i in range(BANKS)]
            deg_ps = ph.enter_context(nc.psum_tensor("deg_ps", [P, WIN], F32))
            degn_ps = ph.enter_context(nc.psum_tensor("degn_ps", [P, TILES], F32))
            dinvT_ps = ph.enter_context(nc.psum_tensor("dinvT_ps", [P, P], F32))
            dn = sb("dn", [P, 4, TILES], F32)
            dinvT = sb("dinvT", [TILES, P], F32)

            b_const, b_ready, b_used, b_free, b_xready, b_xused, b_deg, b_degout, b_n, b_v, b_sq, b_dT, b_dTs, b_dd = (
                sem(n) for n in ("b_const", "b_onehots_ready", "b_onehots_used", "b_bank_free", "b_extra_ready", "b_extra_used",
                                 "b_degrees_summed", "b_degrees_out", "b_degrees_turned", "b_steps", "b_roots",
                                 "b_dinv_turned", "b_dinv_rows", "b_dinv_stored"))

            b_stored = [sem(f"b_window_stored{i}") for i in range(2)]

            def group_bounds(engine, turn):
                _, v = nc.values_load_multi_w_load_instructions(
                    bounds[0:1, bass.ds(turn * (GPI * 2), GPI * 2)], engines=[engine], min_val=0, max_val=EMPTY,
                    skip_runtime_bounds_check_because="a maximum over at most EMPTY chunks, or EMPTY less a count")
                return v

            with nc.Block() as block:
                @block.gpsimd
                def _(pool):
                    nc.gpsimd.iota(iota_f[:, :], [[1, COLS]], base=0, channel_multiplier=0, allow_small_or_imprecise_dtypes=True).then_inc(b_const, 1)
                    nc.gpsimd.iota(g_base[:, :], [[COLS, GROUPS]], base=0, channel_multiplier=0, allow_small_or_imprecise_dtypes=True).then_inc(b_const, 1)
                    nc.gpsimd.memset(stage[:, 1, :, :], 0.0).then_inc(b_const, 1)

                @block.vector
                def _(dve):
                    dve.wait_ge(b_const, 3)
                    nc.vector.memset(ones16[:, :], 1.0).then_inc(b_const, 1)
                    nc.vector.memset(zero16[:, :], 0.0).then_inc(b_const, 1)
                    nc.vector.memset(one32[:, :], 1.0).then_inc(b_const, 1)
                    nc.vector.tensor_copy(iota_col[:, :], iota_f[:, :]).then_inc(b_const, 1)
                    nc.vector.tensor_copy(iota_lane[:, :], iota_f[:, 0:P]).then_inc(b_const, 1)
                    dve.wait_ge(b_const, 8)
                    extras = nc.vector.alloc_register("dve_extras")
                    nc.vector.reg_mov(extras, 1)

                    def one_hots(to_place, to_lane, g, c):
                        nc.vector.tensor_scalar(to_place, iota_col[:, :], g_base[:, bass.ds(g, 1)],
                                                key_col[:, bass.ds(c, 1)], ALU.add, ALU.is_equal)
                        return nc.vector.tensor_scalar(to_lane, iota_lane[:, :], lane_col[:, bass.ds(c, 1)], None, ALU.is_equal)

                    with dve.Fori(0, GROUPS // GPI) as turn:
                        bound = group_bounds(DVE, turn)
                        for u in range(GPI):
                            c0, c1 = bound[2 * u], bound[2 * u + 1]
                            g = turn * GPI + u
                            slot = 2 * u % RING
                            dve.wait_ge(b_used, turn * (2 * GPI) + (2 * u + 1))
                            one_hots(place[:, slot, :], lane[:, slot, :], g, c0).then_inc(b_ready, 1)
                            dve.wait_ge(b_used, turn * (2 * GPI) + (2 * u + 2))
                            one_hots(place[:, slot + 1, :], lane[:, slot + 1, :], g, c0 + 1).then_inc(b_ready, 1)
                            with dve.If(c1 > c0 + 2):
                                with dve.Fori(c0 + 2, c1) as c:
                                    c = nc.s_assert_within(c, 2, CHUNKS - 1)
                                    x = dve.snap(extras)
                                    dve.wait_ge(b_xused, x)
                                    one_hots(place_x[:, :], lane_x[:, :], g, c).then_inc(b_xready, 1)
                                    dve.reg_add(extras, extras, 1)
                            with dve.Else():
                                pass
                    dve.wait_ge(b_n, 1)
                    v = Steps(dve, b_v)
                    v.then(nc.vector.tensor_scalar(dn[:, 0, :], degn_ps[:, :], 1.0, None, ALU.max))
                    nc.vector.reciprocal(dn[:, 1, :], dn[:, 0, :]).then_inc(b_sq, 1)
                    dve.wait_ge(b_sq, 2)
                    v.then(nc.vector.tensor_tensor(dn[:, 3, :], dn[:, 2, :], dn[:, 2, :], ALU.mult))
                    v.then(nc.vector.tensor_tensor(dn[:, 3, :], dn[:, 3, :], dn[:, 0, :], ALU.mult))
                    v.then(nc.vector.tensor_scalar(dn[:, 3, :], dn[:, 3, :], -0.5, 1.5, ALU.mult, ALU.add))
                    v.then(nc.vector.tensor_tensor(dn[:, 3, :], dn[:, 3, :], dn[:, 2, :], ALU.mult))
                    v.then(nc.vector.tensor_scalar(dn[:, 1, :], degn_ps[:, :], 0.0, None, ALU.is_gt))
                    v.then(nc.vector.tensor_tensor(dinv[:, :], dn[:, 3, :], dn[:, 1, :], ALU.mult))
                    dve.wait_ge(b_dT, 1)
                    nc.vector.tensor_copy(dinvT[:, :], dinvT_ps[0:TILES, :]).then_inc(b_dTs, 1)

                @block.tensor
                def _(pe):
                    pe.wait_ge(b_const, 8)
                    extras = nc.tensor.alloc_register("pe_extras")
                    nc.tensor.reg_mov(extras, 1)
                    pe.sem_inc(b_used, RING)
                    pe.sem_inc(b_xused, 1)

                    def degrees_zero(w):
                        pe.wait_ge(b_degout, w + 1)
                        nc.tensor.matmul(deg_ps[0:1, :], ones16[:, :], zero16[:, :], start=True, stop=False, skip_group_check=True)

                    def degrees(buf, tile0):
                        for r in range(TILES // TURNS):
                            m = nc.tensor.matmul(deg_ps[0:1, :], ones16[:, :], stage[:, buf, bass.ds(tile0 + r, 1), :].rearrange("p o n -> p (o n)"),
                                                 start=False, stop=(r == TILES // TURNS - 1), skip_group_check=True)
                        return m

                    with pe.Fori(0, WINS // 2) as pair:
                        for buf in range(2):
                            w = pair * 2 + buf
                            pe.wait_ge(b_free, w * (WIN // G) + BANKS)
                            degrees_zero(w)
                            with pe.Fori(0, TURNS) as t:
                                bound = group_bounds(PE, w * TURNS + t)
                                for u in range(GPI):
                                    c0, c1 = bound[2 * u], bound[2 * u + 1]
                                    g = (w * TURNS + t) * GPI + u
                                    ps, slot = group_ps[u % BANKS], 2 * u % RING
                                    pe.wait_ge(b_free, g + 1)
                                    pe.wait_ge(b_ready, g * 2 + 1)
                                    nc.tensor.matmul(ps[:, :], lane[:, slot, :], place[:, slot, :], start=True, stop=False,
                                                     skip_group_check=True)
                                    with pe.If(c1 > c0 + 2):
                                        with pe.Fori(c0 + 2, c1) as c:
                                            x = pe.snap(extras)
                                            pe.wait_ge(b_ready, g * 2 + 2)
                                            pe.wait_ge(b_xready, x)
                                            nc.tensor.matmul(ps[:, :], lane_x[:, :], place_x[:, :], start=False, stop=False,
                                                             skip_group_check=True).then_inc(b_xused, 1)
                                            pe.reg_add(extras, extras, 1)
                                    with pe.Else():
                                        pass
                                    pe.wait_ge(b_ready, g * 2 + 2)
                                    nc.tensor.matmul(ps[:, :], lane[:, slot + 1, :], place[:, slot + 1, :], start=False, stop=True,
                                                     skip_group_check=True).then_inc(b_used, 2)
                                m = degrees(1 - buf, t * (TILES // TURNS))
                                m.then_inc(b_deg, 1)
                    pe.wait_ge(b_free, GROUPS + BANKS)
                    degrees_zero(WINS)
                    with pe.Fori(0, TURNS) as t:
                        degrees(1, t * (TILES // TURNS)).then_inc(b_deg, 1)
                    pe.wait_ge(b_degout, WINS + 2)
                    for j in range(TILES):
                        m = nc.tensor.matmul(degn_ps[:, j:j + 1], deg_row[0:1, WIN + j * P:WIN + (j + 1) * P], one32[:, :], start=True, stop=True)
                    m.then_inc(b_n, 1)
                    pe.wait_ge(b_v, 7)
                    nc.tensor.transpose(dinvT_ps[0:TILES, :], dinv[:, :], ident[:, :]).then_inc(b_dT, 1)

                @block.scalar
                def _(act):
                    act.sem_inc(b_free, BANKS)
                    act.sem_inc(b_degout, 1)

                    def degrees_out(w):
                        act.wait_ge(b_deg, (w + 1) * TURNS)
                        nc.scalar.activation(deg_row[0:1, bass.ds(w * WIN, WIN)], deg_ps[0:1, :], ACT.Copy).then_inc(b_degout, 1)

                    act.wait_ge(b_const, 8)
                    with act.Fori(0, WINS // 2) as pair:
                        for buf in range(2):
                            w = pair * 2 + buf
                            act.wait_ge(b_stored[buf], pair * 16 + 16)
                            with act.Fori(0, TURNS) as t:
                                for u in range(GPI):
                                    g = (w * TURNS + t) * GPI + u
                                    act.wait_ge(b_used, g * 2 + (2 + RING))
                                    nc.scalar.activation(stage[:, buf, :, bass.ds((t * GPI + u) * G, G)],
                                                         group_ps[u % BANKS][:, :].rearrange("p (d h) -> p h d", d=G), ACT.Copy).then_inc(b_free, 1)
                            degrees_out(w)
                    degrees_out(WINS)
                    act.wait_ge(b_sq, 1)
                    nc.scalar.activation(dn[:, 2, :], dn[:, 1, :], ACT.Sqrt).then_inc(b_sq, 1)

                @block.sync
                def _(sp):
                    for stored in b_stored:
                        sp.sem_inc(stored, 16)
                    with sp.Fori(0, WINS // 2) as pair:
                        for buf in range(2):
                            w = pair * 2 + buf
                            row = sp.snap(w)
                            sp.wait_ge(b_free, (w + 1) * (WIN // G) + BANKS)
                            sp.dma_start(adj_d[bass.ds(row, 1), :, :].rearrange("o p x -> (o p) x"),
                                         stage[:, buf, :, :].rearrange("p h n -> p (h n)")).then_inc(b_stored[buf], 16)
                    for stored in b_stored:
                        sp.wait_ge(stored, 16 * (WINS // 2 + 1))
                    sp.wait_ge(b_dTs, 1)
                    sp.dma_start(dinv_d[:, :], dinvT[:, :]).then_inc(b_dd, 16)
                    sp.wait_ge(b_dd, 16)
        edges.close()
        rest(nc, a, out, sem, keep, ident, dinv, adj_d, dinv_d, xnT_d, root1_d)


def rest(nc, a, out, sem, keep, ident, dinv, adj_d, dinv_d, xnT_d, root1_d):
    def weights(name, shape):
        return keep(name, shape, F32)

    ready = sem("w_loaded")
    mix = keep("mix", [P, 2, D], F32)
    hidden = keep("hidden", [P, 2, NP], F32)
    front = ExitStack()
    split = front.enter_context(nc.sbuf_tensor("split", [P, TILES, 2, D], F16))
    normed = ExitStack()
    xnT = normed.enter_context(nc.sbuf_tensor("xnT", [P, 2, NP], F32))

    with ExitStack() as ph:
        def sb(name, shape, dt=F32):
            return ph.enter_context(nc.sbuf_tensor(name, shape, dt))

        x_all = split[:, :, :, :].rearrange("p j s c -> p (j s c)").bitcast(F32).rearrange("p (j f) -> p j f", f=D)
        xn = sb("xn", [P, SUB, D])
        stats = sb("stats", [P, TILES, 6])
        moments = sb("moments", [P, 2, TILES])
        var = sb("var", [P, TILES])
        inv = sb("inv", [P, TILES])
        root = sb("root", [P, TILES])
        rstd = sb("rstd", [P, TILES])
        shift = sb("shift", [P, TILES])
        tp = [ph.enter_context(nc.psum_tensor(f"n_tp{i}", [P, 2, P], F32)) for i in range(SUB)]
        n_pad, n_in, n_st, n_v, n_sq, n_xn, n_tp, n_out, n_store = (
            sem(n) for n in ("n_padded", "n_loaded", "n_stats", "n_steps", "n_roots", "n_normed", "n_turned", "n_copied", "n_stored"))
        with nc.Block() as block:
            @block.sync
            def _(sp):
                sp.wait_ge(n_pad, 1)
                sp.dma_start(x_all[:, 0:TILES - 1, :], a["x"][0:(TILES - 1) * P, :].rearrange("(j p) f -> p j f", p=P)).then_inc(n_in, 16)
                sp.dma_start(x_all[0:LAST, TILES - 1, :], a["x"][(TILES - 1) * P:N, :]).then_inc(n_in, 16)
                sp.wait_ge(n_out, TILES + SUB)
                sp.dma_start(xnT_d[:, :], xnT[:, :, :].rearrange("p k n -> p (k n)")).then_inc(n_store, 16)
                sp.wait_ge(n_store, 16)

            @block.vector
            def _(dve):
                nc.vector.memset(x_all[:, TILES - 1, :], 0.0).then_inc(n_pad, 1)
                dve.wait_ge(n_in, 32)
                with dve.Fori(0, BATCHES) as i:
                    for u in range(SUB):
                        nc.vector.bn_stats(stats[:, bass.ds(i * SUB + u, 1), :].rearrange("p o s -> p (o s)"),
                                           x_all[:, bass.ds(i * SUB + u, 1), :].rearrange("p o s -> p (o s)")).then_inc(n_st, 1)
                dve.wait_ge(n_st, TILES)
                v = Steps(dve, n_v)
                row_moments(nc, v, moments[:, 0, :], var[:, :], moments[:, 1, :], stats)
                nc.vector.reciprocal(inv[:, :], var[:, :]).then_inc(n_sq, 1)
                dve.wait_ge(n_sq, 2)
                newton(nc, v, rstd[:, :], root[:, :], var[:, :])
                v.then(nc.vector.scalar_tensor_tensor(shift[:, :], moments[:, 0, :], -0.5, rstd[:, :], ALU.mult, ALU.mult))
                with dve.Fori(0, BATCHES) as i:
                    for u in range(SUB):
                        j = i * SUB + u
                        dve.wait_ge(n_tp, j + 1)
                        nc.vector.tensor_scalar(xn[:, u, :], x_all[:, bass.ds(j, 1), :].rearrange("p o s -> p (o s)"), rstd[:, bass.ds(j, 1)],
                                                shift[:, bass.ds(j, 1)], ALU.mult, ALU.add).then_inc(n_xn, 1)

            @block.tensor
            def _(pe):
                pe.sem_inc(n_tp, SUB)
                with pe.Fori(0, BATCHES) as i:
                    for u in range(SUB):
                        j = i * SUB + u
                        pe.wait_ge(n_xn, j + 1)
                        pe.wait_ge(n_out, j + 1)
                        nc.tensor.transpose(tp[u][:, 0, :], xn[:, u, 0:P], ident[:, :])
                        nc.tensor.transpose(tp[u][:, 1, :], xn[:, u, P:D], ident[:, :]).then_inc(n_tp, 1)

            @block.scalar
            def _(act):
                act.sem_inc(n_out, SUB)
                act.wait_ge(n_sq, 1)
                nc.scalar.activation(root[:, :], inv[:, :], ACT.Sqrt).then_inc(n_sq, 1)
                with act.Fori(0, BATCHES) as i:
                    for u in range(SUB):
                        j = i * SUB + u
                        act.wait_ge(n_tp, j + (SUB + 1))
                        nc.scalar.activation(xnT[:, :, bass.ds(j * P, P)], tp[u][:, :, :], ACT.Copy).then_inc(n_out, 1)

    with ExitStack() as ph:
        def sb(name, shape, dt=F32):
            return ph.enter_context(nc.sbuf_tensor(name, shape, dt))

        w_nat = sb("w_nat", [P, 4, 2, D])
        w_kvT = sb("w_kvT", [P, 2, 2 * D])
        w_oT = sb("w_oT", [P, 2, D])
        w_init = sb("w_init", [P, 2, 2, P])
        w_root = sb("w_root", [P, 2, 2, P])
        b_one = sb("b_one", [P, 2])
        ln_g = sb("ln_g", [P, 8, 64])
        ln_b = sb("ln_b", [P, 8, 64])
        xs = sb("xs", [P, SUB, 2, P])
        kv = hidden[:, 0, 0:SUB * 2 * D].rearrange("p (u c) -> p u c", u=SUB)
        sq = hidden[:, 1, 0:SUB * 2 * D]
        HS = SUB * 8
        s1 = sb("s1", [P, 6, HS])
        rt = sb("rt", [P, 2, 2, WIN])
        bd = sb("bd", [P, 2, P])
        t1 = sb("t1", [P, 2, D])
        zero32 = sb("zero32", [P, 2 * P])
        kv_ps = [ph.enter_context(nc.psum_tensor(f"kv_ps{i}", [P, 2 * D], F32)) for i in range(2)]
        h_ps = [ph.enter_context(nc.psum_tensor(f"h_ps{i}", [P, D], F32)) for i in range(2)]
        acc_ps = ph.enter_context(nc.psum_tensor("acc_ps", [P, 2, P], F32))
        r_ps = [ph.enter_context(nc.psum_tensor(f"r_ps{i}", [P, WIN], F32)) for i in range(2)]
        f_z, f_in, f_t, f_tc, f_xs, f_pr, f_kc, f_hf, f_hv, f_v, f_a, f_p, f_kv, f_rt, f_rc, f_rd0, f_rd1, f_m, f_mc = (
            sem(n) for n in ("f_zeroed", "f_loaded", "f_weights_turned", "f_weights_copied", "f_staged", "f_projected", "f_kv_copied",
                             "f_split_done", "f_split_steps", "f_steps", "f_act_steps", "f_pool_steps", "f_kv_summed",
                             "f_root_product", "f_root_copied", "f_root_stored0", "f_root_stored1", "f_mix_product", "f_mix_copied"))
        f_rd = (f_rd0, f_rd1)
        loads = 8 + 4 + 2 + 8 * 2
        with nc.Block() as block:
            @block.sync
            def _(sp):
                for m, name in enumerate(("wk", "wv", "wo", "wq")):
                    w = a[f"L0_mix_{name}"].rearrange("(c p) d -> p c d", p=P)
                    for c in range(2):
                        sp.dma_start(w_nat[:, m, c, :], w[:, c, :]).then_inc(f_in, 16)
                for to, name in ((w_init, "init_w1"), (w_root, "root_w1")):
                    for k in range(2):
                        sp.dma_start(to[:, :, k, :], a[f"L0_gnn_{name}"][k].rearrange("(c f) g -> f c g", f=P)).then_inc(f_in, 16)
                for k in range(2):
                    sp.dma_start(b_one[:, k:k + 1], a["L0_gnn_b1"][k].rearrange("(g o) -> g o", o=1)).then_inc(f_in, 16)
                for h in range(8):
                    kind = "k" if h < 4 else "v"
                    for to, part in ((ln_g, "g"), (ln_b, "b")):
                        sp.dma_start(to[:, h, :], a[f"L0_mix_ln_{kind}_{part}"].rearrange("(o e) -> o e", o=1).broadcast_to([P, 64])).then_inc(f_in, 16)
                with sp.Fori(0, WINS // 2) as pair:
                    for b in range(2):
                        at = sp.snap((pair * 2 + b) * WIN)
                        sp.wait_ge(f_rc, pair * 4 + (2 * b + 4))
                        sp.dma_start(root1_d.rearrange("p (k n) -> p k n", k=2)[:, :, bass.ds(at, WIN)], rt[:, b, :, :]).then_inc(f_rd[b], 16)
                for b in range(2):
                    sp.wait_ge(f_rd[b], 16 * (WINS // 2 + 1))

            @block.gpsimd
            def _(pool):
                def broad(t):
                    return t[:, :, :].rearrange("p h e -> p (h e)").unsqueeze(1).broadcast_to([P, SUB, 2 * D])

                pool.wait_ge(f_in, 16 * loads)
                with pool.Fori(0, BATCHES) as i:
                    for u in range(SUB):
                        j = i * SUB + u
                        pool.wait_ge(f_pr, j + 1)
                        nc.gpsimd.tensor_copy(xs[:, u, :, :], xnT[:, :, bass.ds(j * P, P)]).then_inc(f_xs, 1)
                    pool.wait_ge(f_v, (i + 1) * 9)
                    nc.gpsimd.tensor_tensor(kv[:, :, :], kv[:, :, :], broad(ln_g), ALU.mult).then_inc(f_p, 1)
                    pool.wait_ge(f_p, i * 2 + 1)
                    nc.gpsimd.tensor_tensor(kv[:, :, :], kv[:, :, :], broad(ln_b), ALU.add).then_inc(f_p, 1)

            @block.scalar
            def _(act):
                act.sem_inc(f_kc, 2)
                act.sem_inc(f_rc, 2)
                act.sem_inc(f_rd0, 16)
                act.sem_inc(f_rd1, 16)
                for n in range(3):
                    act.wait_ge(f_t, n + 1)
                    ps = (kv_ps[0], kv_ps[1], r_ps[0])[n]
                    if n < 2:
                        for kc in range(2):
                            ins = nc.scalar.activation(w_kvT[:, kc, n * D:(n + 1) * D], ps[:, kc * D:(kc + 1) * D], ACT.Copy)
                    else:
                        ins = nc.scalar.activation(w_oT[:, 0, :], h_ps[0][:, :], ACT.Copy)
                        ins = nc.scalar.activation(w_oT[:, 1, :], h_ps[1][:, :], ACT.Copy)
                    ins.then_inc(f_tc, 1)
                with act.Fori(0, BATCHES) as i:
                    act.wait_ge(f_kv, i + 1)
                    for u in range(SUB):
                        j = i * SUB + u
                        act.wait_ge(f_pr, j + (SUB + 1))
                        nc.scalar.activation(kv[:, u, :], kv_ps[u % 2][:, :], ACT.Copy).then_inc(f_kc, 1)
                    act.wait_ge(f_v, i * 9 + 3)
                    nc.scalar.activation(sq, kv[:, :, :].rearrange("p u c -> p (u c)"), ACT.Square).then_inc(f_a, 1)
                    act.wait_ge(f_v, i * 9 + 5)
                    nc.scalar.activation(s1[:, 3, :], s1[:, 2, :], ACT.Sqrt).then_inc(f_a, 1)
                with act.Fori(0, WINS // 2) as pair:
                    for b in range(2):
                        act.wait_ge(f_rd[b], pair * 16 + 16)
                        for k in range(2):
                            act.wait_ge(f_rt, pair * 4 + (2 * b + k + 1))
                            nc.scalar.activation(rt[:, b, k, :], r_ps[k][:, :], ACT.Identity, bias=b_one[:, k:k + 1]).then_inc(f_rc, 1)

            @block.vector
            def _(dve):
                nc.vector.memset(zero32[:, :], 0.0).then_inc(f_z, 1)
                nc.vector.memset(bd[:, :, :], 0.0).then_inc(f_z, 1)
                dve.sem_inc(f_hf, 2)
                with dve.Fori(0, BATCHES) as i:
                    for u in range(SUB):
                        j = i * SUB + u
                        dve.wait_ge(f_pr, j + (SUB + 1))
                        hi = split[:, bass.ds(j, 1), 0, :].rearrange("p o c -> p (o c)")
                        lo = split[:, bass.ds(j, 1), 1, :].rearrange("p o c -> p (o c)")
                        nc.vector.tensor_scalar(hi, h_ps[u % 2][:, :], dinv[:, bass.ds(j, 1)], None, ALU.mult).then_inc(f_hv, 1)
                        dve.wait_ge(f_hv, j + 1)
                        nc.vector.scalar_tensor_tensor(lo, h_ps[u % 2][:, :], dinv[:, bass.ds(j, 1)], hi, ALU.mult, ALU.subtract).then_inc(f_hf, 1)
                    dve.wait_ge(f_kc, (i + 1) * SUB + 2)
                    v = Steps(dve, f_v, i * 9)
                    rows = kv[:, :, :].rearrange("p u (h e) -> p (u h) e", e=64)

                    def each(k):
                        return s1[:, k, :].unsqueeze(2).broadcast_to([P, HS, 64])

                    v.then(nc.vector.tensor_reduce(s1[:, 0, :], rows, X, ALU.add))
                    v.then(nc.vector.tensor_scalar(s1[:, 0, :], s1[:, 0, :], -1.0 / 64, None, ALU.mult))
                    v.then(nc.vector.tensor_tensor(rows, rows, each(0), ALU.add))
                    dve.wait_ge(f_a, i * 2 + 1)
                    v.then(nc.vector.tensor_reduce(s1[:, 1, :], sq.rearrange("p (h e) -> p h e", e=64), X, ALU.add))
                    nc.vector.tensor_scalar(s1[:, 1, :], s1[:, 1, :], 1.0 / 64, EPS, ALU.mult, ALU.add).then_inc(f_z, 1)
                    dve.wait_ge(f_z, i + 3)
                    v.then(nc.vector.reciprocal(s1[:, 2, :], s1[:, 1, :]))
                    dve.wait_ge(f_a, i * 2 + 2)
                    v.then(nc.vector.tensor_tensor(s1[:, 4, :], s1[:, 3, :], s1[:, 3, :], ALU.mult))
                    v.then(nc.vector.scalar_tensor_tensor(s1[:, 4, :], s1[:, 4, :], -0.5, s1[:, 1, :], ALU.mult, ALU.mult))
                    v.then(nc.vector.scalar_tensor_tensor(s1[:, 5, :], s1[:, 4, :], 1.5, s1[:, 3, :], ALU.add, ALU.mult))
                    v.then(nc.vector.tensor_tensor(rows, rows, each(5), ALU.mult))
                dve.wait_ge(f_kv, BATCHES + 1)
                for c in range(2):
                    for h in range(2):
                        q = slice(64 * h, 64 * h + 64)
                        nc.vector.tensor_scalar(bd[q, c, q], acc_ps[q, c, q], 1.0 / N, None, ALU.mult).then_inc(f_mc, 1)
                for c in range(2):
                    dve.wait_ge(f_m, c + 1)
                    nc.vector.tensor_copy(t1[:, c, :], h_ps[c][:, :]).then_inc(f_mc, 1)
                for c in range(2):
                    dve.wait_ge(f_m, c + 3)
                    nc.vector.tensor_copy(mix[:, c, :], kv_ps[c][:, 0:D]).then_inc(f_mc, 1)

            @block.tensor
            def _(pe):
                pe.wait_ge(f_in, 16 * loads)
                pe.wait_ge(f_z, 2)
                for n in range(3):
                    for oc in range(2):
                        for kc in range(2):
                            if n < 2:
                                to = kv_ps[n][:, kc * D + oc * P:kc * D + (oc + 1) * P]
                            else:
                                to = h_ps[kc][:, oc * P:(oc + 1) * P]
                            t = nc.tensor.transpose(to, w_nat[:, n, oc, kc * P:(kc + 1) * P], ident[:, :])
                    t.then_inc(f_t, 1)
                pe.wait_ge(f_tc, 3)
                nc.tensor.matmul(acc_ps[:, :, :].rearrange("p c e -> p (c e)"), zero32[:, 0:P], zero32[:, :], start=True, stop=False, skip_group_check=True)
                pe.sem_inc(f_pr, SUB)
                pe.sem_inc(f_kv, 1)

                def products(base, count, last):
                    for u in range(count):
                        rows = LAST if last and u == count - 1 else P
                        for c in range(2):
                            m = nc.tensor.matmul(acc_ps[:, c, :], kv[0:rows, u, c * P:(c + 1) * P], kv[0:rows, u, D + c * P:D + (c + 1) * P],
                                                 start=False, stop=last and u == count - 1, skip_group_check=True)
                    m.then_inc(f_kv, 1)

                def project(i):
                    for u in range(SUB):
                        j = i * SUB + u
                        pe.wait_ge(f_xs, j + 1)
                        pe.wait_ge(f_kc, j + 1)
                        pe.wait_ge(f_hf, j + 1)
                        for k in range(2):
                            nc.tensor.matmul(kv_ps[u % 2][:, :], xs[:, u, k, :], w_kvT[:, k, :], start=(k == 0), stop=(k == 1))
                        for k in range(2):
                            m = nc.tensor.matmul(h_ps[u % 2][:, :], xs[:, u, k, :], w_init[:, k, :, :].rearrange("p s g -> p (s g)"),
                                                 start=(k == 0), stop=(k == 1))
                        m.then_inc(f_pr, 1)

                with pe.Fori(0, BATCHES - 1) as i:
                    project(i)
                    pe.wait_ge(f_p, i * 2 + 2)
                    products(i, SUB, False)
                project(BATCHES - 1)
                pe.wait_ge(f_p, 2 * BATCHES)
                products(BATCHES - 1, SUB, True)
                with pe.Fori(0, WINS) as w:
                    for s in range(2):
                        pe.wait_ge(f_rc, w * 2 + (s + 1))
                        for k in range(2):
                            m = nc.tensor.matmul(r_ps[s][:, :], w_root[:, k, s, :], xnT[:, k, bass.ds(w * WIN, WIN)], start=(k == 0), stop=(k == 1))
                        m.then_inc(f_rt, 1)
                pe.wait_ge(f_mc, 4)
                for c in range(2):
                    nc.tensor.matmul(h_ps[c][:, :], bd[:, c, :], w_nat[:, 3, c, :], start=True, stop=True).then_inc(f_m, 1)
                pe.wait_ge(f_mc, 6)
                for d in range(2):
                    for c in range(2):
                        m = nc.tensor.matmul(kv_ps[d][:, 0:D], t1[:, c, d * P:(d + 1) * P], w_oT[:, c, :], start=(c == 0), stop=(c == 1))
                    m.then_inc(f_m, 1)
    normed.close()

    dinv_b = front.enter_context(nc.sbuf_tensor("dinv_b", [P, NP], F32))
    b_in = sem("dinv_b_in")

    p_in = [sem(f"p_piece_in{i}") for i in range(PIECES)]
    p_free = [sem(f"p_piece_used{i}") for i in range(PIECES)]
    p_rin = [sem(f"p_root_in{i}") for i in range(2)]
    p_accs = [sem(f"p_acc_read{i}") for i in range(2)]
    p_vs = [sem(f"p_steps{i}") for i in range(2)]
    q_st, q_pr, q_hi, q_lo = (sem(f"q_{n}") for n in ("staged", "projected", "high", "low"))

    def propagate(name, blocks, root_tile, run, again):
        streamed = root_tile is None
        with ExitStack() as ph:
            ring = ph.enter_context(nc.sbuf_tensor(f"{name}_ring", [P, PIECES, PT, WIN], F16))
            rin = ph.enter_context(nc.sbuf_tensor(f"{name}_rin", [P, 2, 2, WIN], F32)) if streamed else None
            tmp = ph.enter_context(nc.sbuf_tensor(f"{name}_tmp", [P, 2, WIN], F32))
            acc = [[ph.enter_context(nc.psum_tensor(f"{name}_acc{b}{k}", [P, WIN], F32)) for k in range(blocks)] for b in range(2)]
            p_acc, p_v = p_accs[blocks - 1], p_vs[blocks - 1]
            windows = run * WINS
            reads = again * WINS * blocks
            with nc.Block() as block:
                @block.sync
                def _(sp):
                    if run == 0:
                        sp.dma_start(dinv_b[:, :], dinv_d.rearrange("h (o p) -> o (h p)", o=1).broadcast_to([P, NP])).then_inc(b_in, 16)
                    with sp.Fori(0, WINS // 2) as pair:
                        for b in range(2):
                            w = sp.snap(pair * 2 + b)
                            if streamed:
                                at = sp.snap(w * WIN)
                                sp.wait_ge(p_acc, pair * 4 + (reads + 2 * b + 2))
                                sp.dma_start(rin[:, b, :, :], root1_d.rearrange("p (k n) -> p k n", k=2)[:, :, bass.ds(at, WIN)]).then_inc(p_rin[b], 16)
                            for i in range(PIECES):
                                sp.wait_ge(p_free[i], pair * 2 + (windows + b + 1))
                                sp.dma_start(ring[:, i, :, :].rearrange("p t n -> p (t n)"),
                                             adj_d[bass.ds(w, 1), :, i * PT * WIN:(i + 1) * PT * WIN].rearrange("o p x -> (o p) x")).then_inc(p_in[i], 16)

                @block.tensor
                def _(pe):
                    if run == 0:
                        for s in p_free:
                            pe.sem_inc(s, 1)
                    with pe.Fori(0, WINS // 2) as pair:
                        for b in range(2):
                            pe.wait_ge(p_acc, pair * (2 * blocks) + (reads + (b + 1) * blocks))
                            for i in range(PIECES):
                                pe.wait_ge(p_in[i], pair * 32 + 16 * (windows + b + 1))
                                for t in range(PT):
                                    h = i * PT + t
                                    for k in range(blocks):
                                        for part in range(2):
                                            m = nc.tensor.matmul(acc[b][k][:, :], split[:, h, part, k * P:(k + 1) * P], ring[:, i, t, :],
                                                                 start=(h == 0 and part == 0), stop=(h == TILES - 1 and part == 1))
                                m.then_inc(p_free[i], 1)

                @block.vector
                def _(dve):
                    if again == 0:
                        dve.sem_inc(p_acc, 2 * blocks)
                    dve.wait_ge(b_in, 16)
                    with dve.Fori(0, WINS // 2) as pair:
                        v = Steps(dve, p_v, pair * (4 * blocks) + 2 * reads)
                        for b in range(2):
                            w = pair * 2 + b
                            dve.wait_ge(p_free[PIECES - 1], w + (windows + 2))
                            if streamed:
                                dve.wait_ge(p_rin[b], pair * 16 + 16 * (again * (WINS // 2) + 1))
                            for k in range(blocks):
                                one = tmp[:, (b * blocks + k) % 2, :]
                                v.then(nc.vector.tensor_tensor(one, acc[b][k][:, :], dinv_b[:, bass.ds(w * WIN, WIN)], ALU.mult))
                                add = rin[:, b, k, :] if streamed else root_tile[:, bass.ds(w * WIN, WIN)]
                                v.then(nc.vector.tensor_tensor(one, one, add, ALU.add))
                                nc.vector.tensor_scalar(hidden[:, k, bass.ds(w * WIN, WIN)], one, 0.0, None, ALU.max).then_inc(p_acc, 1)

    def project(name, width, terms, run):
        stacks = 1 + max(t[0] for t in terms)
        with ExitStack() as ph:
            hs = ph.enter_context(nc.sbuf_tensor(f"{name}_hs", [P, SUB, 2, P], F32))
            ps = [ph.enter_context(nc.psum_tensor(f"{name}_ps{i}", [P, D], F32)) for i in range(SUB)]
            tiles = run * TILES
            with nc.Block() as block:
                @block.gpsimd
                def _(pool):
                    with pool.Fori(0, BATCHES) as i:
                        for u in range(SUB):
                            j = i * SUB + u
                            pool.wait_ge(q_pr, j + (tiles + 1))
                            nc.gpsimd.tensor_copy(hs[:, u, 0:stacks, :], hidden[:, 0:stacks, bass.ds(j * P, P)]).then_inc(q_st, 1)

                @block.tensor
                def _(pe):
                    if run == 0:
                        pe.sem_inc(q_pr, SUB)
                    with pe.Fori(0, BATCHES) as i:
                        for u in range(SUB):
                            j = i * SUB + u
                            pe.wait_ge(q_st, j + (tiles + 1))
                            pe.wait_ge(q_lo, j + (tiles + 1))
                            for k, w, at, stop, start in terms:
                                m = nc.tensor.matmul(ps[u][:, at:at + P], hs[:, u, k, :], w, start=start, stop=stop)
                            m.then_inc(q_pr, 1)

                @block.vector
                def _(dve):
                    if run == 0:
                        dve.sem_inc(q_lo, SUB)
                    with dve.Fori(0, BATCHES) as i:
                        for u in range(SUB):
                            j = i * SUB + u
                            dve.wait_ge(q_pr, j + (tiles + SUB + 1))
                            hi = split[:, bass.ds(j, 1), 0, 0:width].rearrange("p o c -> p (o c)")
                            lo = split[:, bass.ds(j, 1), 1, 0:width].rearrange("p o c -> p (o c)")
                            nc.vector.tensor_scalar(hi, ps[u][:, 0:width], dinv[:, bass.ds(j, 1)], None, ALU.mult).then_inc(q_hi, 1)
                            dve.wait_ge(q_hi, j + (tiles + 1))
                            nc.vector.scalar_tensor_tensor(lo, ps[u][:, 0:width], dinv[:, bass.ds(j, 1)], hi, ALU.mult, ALU.subtract).then_inc(q_lo, 1)

    conv = ExitStack()
    w_one = conv.enter_context(nc.sbuf_tensor("w_one", [P, 2, P], F32))
    w_two0 = conv.enter_context(nc.sbuf_tensor("w_two0", [P, P], F32))
    w_two = conv.enter_context(nc.sbuf_tensor("w_two", [P, P], F32))
    w_rtwo = conv.enter_context(nc.sbuf_tensor("w_rtwo", [P, P], F32))
    b_two = conv.enter_context(nc.sbuf_tensor("b_two", [P, 1], F32))
    H = P // 2
    c_z, c_in = sem("c_zeroed"), sem("c_loaded")
    with nc.Block() as block:
        @block.sync
        def _(sp):
            sp.dma_start(w_one[:, :, :], a["L0_gnn_w1"].rearrange("k f g -> f k g")).then_inc(c_in, 16)
            sp.wait_ge(c_z, 1)
            for k in range(2):
                q = slice(H * k, H * k + H)
                sp.dma_start(w_two0[:, q], a["L0_gnn_init_w2"][k]).then_inc(c_in, 16)
                sp.dma_start(w_rtwo[:, q], a["L0_gnn_root_w2"][k]).then_inc(c_in, 16)
                sp.dma_start(w_two[q, q], a["L0_gnn_w2"][k]).then_inc(c_in, 16)
                sp.dma_start(b_two[q, :], a["L0_gnn_b2"][k].rearrange("(g o) -> g o", o=1)).then_inc(c_in, 16)
            sp.wait_ge(c_in, 16 * 9)

        @block.vector
        def _(dve):
            nc.vector.memset(w_two[:, :], 0.0).then_inc(c_z, 1)
            dve.wait_ge(c_in, 16 * 9)
            nc.vector.tensor_scalar(w_two0[:, :], w_two0[:, :], 0.5, None, ALU.mult).then_inc(c_z, 1)
            nc.vector.tensor_scalar(w_rtwo[:, :], w_rtwo[:, :], 0.5, None, ALU.mult).then_inc(c_z, 1)
            dve.wait_ge(c_z, 3)

    propagate("a0", 2, None, 0, 0)
    for t in (1, 2):
        project(f"a{t}p", D, [(0, w_one[:, 0, :], 0, True, True), (1, w_one[:, 1, :], P, True, True)], t - 1)
        propagate(f"a{t}", 2, None, t, t)
    with nc.sbuf_tensor("root_two", [P, NP], F32) as root_two:
        with ExitStack() as ph:
            r2 = [ph.enter_context(nc.psum_tensor(f"r2_ps{i}", [P, WIN], F32)) for i in range(2)]
            r_pr, r_cp = sem("r2_projected"), sem("r2_copied")
            with nc.Block() as block:
                @block.tensor
                def _(pe):
                    with pe.Fori(0, WINS // 2) as pair:
                        for b in range(2):
                            pe.wait_ge(r_cp, pair * 2 + (b + 1))
                            for k in range(2):
                                m = nc.tensor.matmul(r2[b][:, :], w_rtwo[:, :], hidden[:, k, bass.ds((pair * 2 + b) * WIN, WIN)], start=(k == 0), stop=(k == 1))
                            m.then_inc(r_pr, 1)

                @block.scalar
                def _(act):
                    act.sem_inc(r_cp, 2)
                    with act.Fori(0, WINS // 2) as pair:
                        for b in range(2):
                            act.wait_ge(r_pr, pair * 2 + (b + 1))
                            nc.scalar.activation(root_two[:, bass.ds((pair * 2 + b) * WIN, WIN)], r2[b][:, :], ACT.Identity, bias=b_two[:, :]).then_inc(r_cp, 1)

        project("b0p", P, [(0, w_two0[:, :], 0, False, True), (1, w_two0[:, :], 0, True, False)], 2)
        propagate("b0", 1, root_two, 3, 0)
        for t in (1, 2):
            project(f"b{t}p", P, [(0, w_two[:, :], 0, True, True)], 2 + t)
            propagate(f"b{t}", 1, root_two, 3 + t, t)
    conv.close()

    front.close()
    final(nc, a, out, sem, ident, mix, hidden, xnT_d)


def row_moments(nc, v, twice_mean, var, diff, stats):
    tt = nc.vector.tensor_tensor
    v.then(tt(twice_mean, stats[:, :, 1], stats[:, :, 4], ALU.add))
    v.then(tt(diff, stats[:, :, 1], stats[:, :, 4], ALU.subtract))
    v.then(tt(var, stats[:, :, 2], stats[:, :, 5], ALU.add))
    v.then(tt(diff, diff, diff, ALU.mult))
    v.then(nc.vector.tensor_scalar(var, var, 1.0 / D, EPS, ALU.mult, ALU.add))
    v.then(nc.vector.scalar_tensor_tensor(var, diff, 0.25, var, ALU.mult, ALU.add))


def newton(nc, v, to, root, var):
    v.then(nc.vector.tensor_tensor(to, root, root, ALU.mult))
    v.then(nc.vector.scalar_tensor_tensor(to, to, -0.5, var, ALU.mult, ALU.mult))
    v.then(nc.vector.scalar_tensor_tensor(to, to, 1.5, root, ALU.add, ALU.mult))


def final(nc, a, out, sem, ident, mix, hidden, xnT_d):
    HB = 2
    EXP = EXPERTS
    with ExitStack() as ph:
        def sb(name, shape, dt=F32):
            return ph.enter_context(nc.sbuf_tensor(name, shape, dt))

        fc1 = sb("fc1", [P, P])
        fc1_b = sb("fc1_b", [P, 1])
        fc2 = sb("fc2", [P, D])
        bias = sb("bias", [P, 2, D])
        rw1 = sb("rw1", [P, 2, P])
        rb1 = sb("rb1", [P, 1])
        rw2 = sb("rw2", [P, EXP])
        rb2 = sb("rb2", [P, EXP])
        ew = [sb(f"ew{n}", [P, EXP, 2, D]) for n in range(3)]
        eb = [sb(f"eb{n}", [P, EXP, 2]) for n in range(2)]
        eb3 = sb("eb3", [EXP, D])
        iota6 = sb("iota6", [P, SUB, EXP])
        xt = sb("xt", [P, SUB, D])
        xT = sb("xT", [P, 2, ROW])
        dT = sb("dT", [P, ROW])
        x2 = sb("x2", [P, SUB, D])
        xl = sb("xl", [P, SUB, D])
        xlT = sb("xlT", [P, 2, ROW])
        rhT = sb("rhT", [P, ROW])
        h1 = sb("h1", [P, 2, ROW])
        h2 = sb("h2", [P, 2, ROW])
        stats = sb("f_stats", [P, SUB, 6])
        mom = sb("f_mom", [P, 2, SUB])
        m7 = sb("m7", [P, 8, SUB])
        lg = sb("lg", [P, SUB, EXP])
        pr = sb("pr", [P, SUB, EXP])
        t6 = sb("t6", [P, SUB, EXP])
        one1 = sb("one1", [P, SUB, EXP])
        one2 = sb("one2", [P, SUB, EXP])
        rw = sb("rw", [P, SUB, EXP])
        rwT = sb("rwT", [EXP, ROW])
        WIDE, SLIM = 4, 3
        wide = [ph.enter_context(nc.psum_tensor(f"wide{i}", [P, WIN], F32)) for i in range(WIDE)]
        slim = [ph.enter_context(nc.psum_tensor(f"slim{i}", [P, 512], F32)) for i in range(SLIM)]
        w_full = [sem(f"wide_full{i}") for i in range(WIDE)]
        w_empty = [sem(f"wide_empty{i}") for i in range(WIDE)]
        s_full = [sem(f"slim_full{i}") for i in range(SLIM)]
        s_empty = [sem(f"slim_empty{i}") for i in range(SLIM)]
        l_in, l_xt, l_xT, l_pool, l_v, l_sq, l_xln, l_lg, l_ex, l_out, l_xfree, l_rw = (
            sem(n) for n in ("l_weights", "l_x_in", "l_xT_in", "l_pool", "l_steps", "l_roots", "l_normed", "l_logits", "l_exps",
                             "l_stored", "l_x_used", "l_routing"))

        order_w = [("d", h) for h in range(HB)] + [("r", h) for h in range(HB)]
        for e in range(EXP):
            order_w += [("1", e, hc, h) for hc in range(2) for h in range(HB)] + [("2", e, hc, h) for hc in range(2) for h in range(HB)]
        order_s = [("rec", u) for u in range(SUB)] + [("turn", u) for u in range(SUB)] + [("logit", 0)]
        order_s += [("rwT", 0), ("rwT", 1)] + [("b3", u) for u in range(SUB)]
        order_s += [("3", e, u) for e in range(EXP) for u in range(SUB)]
        assert len(order_w) % WIDE == 0 and len(order_s) % SLIM == 0

        def bank_of(key, i):
            if key in order_w:
                n, per, kind = order_w.index(key), WIDE, (wide, w_full, w_empty)
                total = len(order_w)
            else:
                n, per, kind = order_s.index(key), SLIM, (slim, s_full, s_empty)
                total = len(order_s)
            b = n % per
            return kind[0][b], kind[1][b], kind[2][b], i * (total // per) + (n // per + 1)

        def fill(pe, key, i):
            ps, full, empty, turn = bank_of(key, i)
            pe.wait_ge(empty, turn)
            return ps, full

        def take(eng, key, i):
            ps, full, empty, turn = bank_of(key, i)
            eng.wait_ge(full, turn)
            return ps, empty

        def drained(eng, key, i):
            _, _, empty, turn = bank_of(key, i)
            eng.wait_ge(empty, turn + 1)

        loads = 12 + 7 * EXP
        V = 37
        with nc.Block() as block:
            @block.sync
            def _(sp):
                def column(name):
                    return a[name].rearrange("(g o) -> g o", o=1)

                def row(name, n):
                    return a[name].rearrange("(o g) -> o g", o=1).broadcast_to([P, n])

                for k in range(2):
                    sp.dma_start(fc1[64 * k:64 * k + 64, :], a["L0_gnn_fc1_w"][:, :]).then_inc(l_in, 16)
                    sp.dma_start(rw1[:, k, :], a["L0_ffn_router_w1"][k * P:(k + 1) * P, :]).then_inc(l_in, 16)
                for to, of in ((fc1_b, column("L0_gnn_fc1_b")), (rb1, column("L0_ffn_router_b1")), (fc2, a["L0_gnn_fc2_w"]),
                               (rw2, a["L0_ffn_router_w2"]), (rb2, row("L0_ffn_router_b2", EXP)), (eb3, a["L0_ffn_expert_b3"])):
                    sp.dma_start(to[:, :], of).then_inc(l_in, 16)
                sp.dma_start(bias[:, 0, :], row("L0_gnn_fc2_b", D)).then_inc(l_in, 16)
                sp.dma_start(bias[:, 1, :], row("L0_mix_bo", D)).then_inc(l_in, 16)
                for e in range(EXP):
                    for n in range(3):
                        sp.dma_start(ew[n][:, e, :, :], a[f"L0_ffn_expert_w{n + 1}"][e].rearrange("(c p) h -> p c h", p=P)).then_inc(l_in, 16)
                    for n in range(2):
                        for c in range(2):
                            sp.dma_start(eb[n][:, e, c:c + 1], a[f"L0_ffn_expert_b{n + 1}"][e, c * P:(c + 1) * P].rearrange("(p o) -> p o", o=1)).then_inc(l_in, 16)

                def load(i, rows):
                    at = sp.snap(i * ROW) if i is not BATCHES - 1 else (BATCHES - 1) * ROW
                    sp.wait_ge(l_xfree, i + 1)
                    sp.dma_start(xt[:, 0:SUB - 1, :], a["x"][bass.ds(at, (SUB - 1) * P), :].rearrange("(j p) f -> p j f", p=P)).then_inc(l_xt, 16)
                    sp.dma_start(xt[0:rows, SUB - 1, :], a["x"][bass.ds(at + (SUB - 1) * P, rows), :]).then_inc(l_xt, 16)

                def loadT(i):
                    sp.dma_start(xT[:, :, :], xnT_d.rearrange("p (k n) -> p k n", k=2)[:, :, bass.ds(i * ROW, ROW)]).then_inc(l_xT, 16)

                def store(i, rows):
                    at = sp.snap(i * ROW) if i is not BATCHES - 1 else (BATCHES - 1) * ROW
                    for u in range(SUB - SLIM, SUB):
                        drained(sp, ("3", EXP - 1, u), i)
                    sp.dma_start(out[bass.ds(at, (SUB - 1) * P), :].rearrange("(j p) f -> p j f", p=P), x2[:, 0:SUB - 1, :]).then_inc(l_out, 16)
                    sp.dma_start(out[bass.ds(at + (SUB - 1) * P, rows), :], x2[0:rows, SUB - 1, :]).then_inc(l_out, 16)

                with sp.Fori(0, BATCHES - 1) as i:
                    load(i, P)
                    loadT(i)
                    store(i, P)
                load(BATCHES - 1, LAST)
                loadT(BATCHES - 1)
                store(BATCHES - 1, LAST)
                sp.wait_ge(l_out, 32 * (BATCHES + 1))

            @block.gpsimd
            def _(pool):
                nc.gpsimd.iota(iota6[:, :, :], [[0, SUB], [1, EXP]], base=-EXP, channel_multiplier=0, allow_small_or_imprecise_dtypes=True).then_inc(l_pool, 1)

            @block.scalar
            def _(act):
                act.wait_ge(l_in, 16 * loads)
                for s in w_empty + s_empty:
                    act.sem_inc(s, 1)
                with act.Fori(0, BATCHES) as i:
                    def relu(key, to, b):
                        ps, empty = take(act, key, i)
                        nc.scalar.activation(to, ps[:, 0:WIN], ACT.Relu, bias=b).then_inc(empty, 1)

                    def layer(n, e):
                        for hc in range(2):
                            for h in range(HB):
                                relu((n, e, hc, h), (h1 if n == "1" else h2)[:, hc, h * WIN:(h + 1) * WIN], eb[int(n) - 1][:, e, hc:hc + 1])

                    for h in range(HB):
                        relu(("d", h), dT[:, h * WIN:(h + 1) * WIN], fc1_b[:, :])
                    act.wait_ge(l_sq, i * 2 + 1)
                    nc.scalar.activation(m7[:, 2, :], m7[:, 1, :], ACT.Sqrt).then_inc(l_sq, 1)
                    for u in range(SUB):
                        ps, empty = take(act, ("turn", u), i)
                        nc.scalar.activation(xlT[:, :, u * P:(u + 1) * P], ps[:, 0:D].rearrange("p (k n) -> p k n", k=2), ACT.Copy).then_inc(empty, 1)
                    for h in range(HB):
                        relu(("r", h), rhT[:, h * WIN:(h + 1) * WIN], rb1[:, :])
                    act.wait_ge(l_lg, i * 2 + 1)
                    nc.scalar.activation(pr[:, :, :], lg[:, :, :], ACT.Exp).then_inc(l_ex, 1)
                    act.wait_ge(l_lg, i * 2 + 2)
                    nc.scalar.activation(m7[:, 4, :], m7[:, 6, :], ACT.Exp).then_inc(l_ex, 1)
                    layer("1", 0)
                    layer("2", 0)
                    for g in range(2):
                        ps, empty = take(act, ("rwT", g), i)
                        w = min(4, SUB - 4 * g) * P
                        nc.scalar.activation(rwT[:, 4 * g * P:4 * g * P + w], ps[0:EXP, 0:w], ACT.Copy).then_inc(empty, 1)
                    for e in range(1, EXP):
                        layer("1", e)
                        layer("2", e)

            @block.vector
            def _(dve):
                dve.wait_ge(l_in, 16 * loads)
                v0 = Steps(dve, l_v)
                v0.done(nc.vector.memset(xt[:, SUB - 1, :], 0.0))
                v0.done(nc.vector.tensor_scalar(fc1[:, :], fc1[:, :], 0.5, None, ALU.mult))
                v0.then(nc.vector.tensor_tensor(bias[:, 0, :], bias[:, 0, :], bias[:, 1, :], ALU.add))
                dve.wait_ge(l_pool, 1)
                dve.sem_inc(l_xfree, 1)
                dve.sem_inc(l_out, 32)
                with dve.Fori(0, BATCHES) as i:
                    v = Steps(dve, l_v, i * V + 3)
                    tt, red = nc.vector.tensor_tensor, nc.vector.tensor_reduce

                    def every(k):
                        return m7[:, k, :].unsqueeze(2).broadcast_to([P, SUB, EXP])

                    def first_of(to, value):
                        v.then(tt(to[:, :, :], t6[:, :, :], every(value), ALU.is_equal))
                        v.then(tt(to[:, :, :], to[:, :, :], iota6[:, :, :], ALU.mult))
                        v.then(red(m7[:, 6, :], to[:, :, :], X, ALU.min))
                        v.then(tt(to[:, :, :], iota6[:, :, :], every(6), ALU.is_equal))

                    dve.wait_ge(l_xt, i * 32 + 32)
                    dve.wait_ge(l_out, i * 32 + 32)
                    tt(x2[:, :, :], xt[:, :, :], bias[:, 0, :].unsqueeze(1).broadcast_to([P, SUB, D]), ALU.add).then_inc(l_xfree, 1)
                    dve.wait_ge(l_xfree, i + 2)
                    for u in range(SUB):
                        ps, empty = take(dve, ("rec", u), i)
                        tt(x2[:, u, :], x2[:, u, :], ps[:, 0:D], ALU.add).then_inc(empty, 1)
                    for u in range(SUB):
                        drained(dve, ("rec", u), i)
                        v.done(nc.vector.bn_stats(stats[:, u, :], x2[:, u, :]))
                    v.settle()
                    row_moments(nc, v, mom[:, 0, :], m7[:, 0, :], mom[:, 1, :], stats)
                    nc.vector.reciprocal(m7[:, 1, :], m7[:, 0, :]).then_inc(l_sq, 1)
                    dve.wait_ge(l_sq, i * 2 + 2)
                    newton(nc, v, m7[:, 3, :], m7[:, 2, :], m7[:, 0, :])
                    v.then(nc.vector.scalar_tensor_tensor(m7[:, 4, :], mom[:, 0, :], -0.5, m7[:, 3, :], ALU.mult, ALU.mult))
                    for u in range(SUB):
                        nc.vector.tensor_scalar(xl[:, u, :], x2[:, u, :], m7[:, 3, u:u + 1], m7[:, 4, u:u + 1], ALU.mult, ALU.add).then_inc(l_xln, 1)
                    dve.wait_ge(l_xln, i * SUB + SUB)
                    ps, empty = take(dve, ("logit", 0), i)
                    tt(lg[:, :, :], ps[:, 0:SUB * EXP].rearrange("p (u e) -> p u e", e=EXP), rb2[:, :].unsqueeze(1).broadcast_to([P, SUB, EXP]), ALU.add).then_inc(empty, 1)
                    drained(dve, ("logit", 0), i)
                    v.then(red(m7[:, 5, :], lg[:, :, :], X, ALU.max))
                    tt(lg[:, :, :], lg[:, :, :], every(5), ALU.subtract).then_inc(l_lg, 1)
                    dve.wait_ge(l_ex, i * 2 + 1)
                    v.then(red(m7[:, 6, :], pr[:, :, :], X, ALU.add))
                    v.then(nc.vector.reciprocal(m7[:, 7, :], m7[:, 6, :]))
                    v.then(tt(t6[:, :, :], pr[:, :, :], every(7), ALU.mult))
                    v.then(red(m7[:, 5, :], t6[:, :, :], X, ALU.max))
                    first_of(one1, 5)
                    v.then(nc.vector.scalar_tensor_tensor(t6[:, :, :], one1[:, :, :], -4.0, t6[:, :, :], ALU.mult, ALU.add))
                    v.then(red(m7[:, 7, :], t6[:, :, :], X, ALU.max))
                    first_of(one2, 7)
                    tt(m7[:, 6, :], m7[:, 7, :], m7[:, 5, :], ALU.subtract).then_inc(l_lg, 1)
                    dve.wait_ge(l_ex, i * 2 + 2)
                    v.then(nc.vector.tensor_scalar(m7[:, 1, :], m7[:, 4, :], 1.0, None, ALU.add))
                    v.then(nc.vector.reciprocal(m7[:, 3, :], m7[:, 1, :]))
                    v.then(tt(m7[:, 0, :], m7[:, 4, :], m7[:, 3, :], ALU.mult))
                    v.then(tt(one1[:, :, :], one1[:, :, :], every(3), ALU.mult))
                    v.then(tt(one2[:, :, :], one2[:, :, :], every(0), ALU.mult))
                    tt(rw[:, :, :], one1[:, :, :], one2[:, :, :], ALU.add).then_inc(l_rw, 1)
                    dve.wait_ge(l_rw, i + 1)
                    for u in range(SUB):
                        ps, empty = take(dve, ("b3", u), i)
                        tt(x2[:, u, :], x2[:, u, :], ps[:, 0:D], ALU.add).then_inc(empty, 1)
                    for e in range(EXP):
                        for u in range(SUB):
                            drained(dve, ("b3", u) if e == 0 else ("3", e - 1, u), i)
                            ps, empty = take(dve, ("3", e, u), i)
                            nc.vector.scalar_tensor_tensor(x2[:, u, :], ps[:, 0:D], rw[:, u, e:e + 1], x2[:, u, :], ALU.mult, ALU.add).then_inc(empty, 1)
                    assert v.n == V, v.n

            @block.tensor
            def _(pe):
                pe.wait_ge(l_v, 3)
                with pe.Fori(0, BATCHES) as i:
                    mm = nc.tensor.matmul

                    def dense(n, e, weights, rows):
                        for hc in range(2):
                            for h in range(HB):
                                ps, full = fill(pe, (n, e, hc, h), i)
                                for c in range(2):
                                    if n == "2":
                                        drained(pe, ("1", e, c, h), i)
                                    m = mm(ps[:, :], weights[:, e, c, hc * P:(hc + 1) * P], rows[:, c, h * WIN:(h + 1) * WIN], start=(c == 0), stop=(c == 1))
                                m.then_inc(full, 1)

                    def last_layer(e):
                        for c in range(2):
                            for h in range(HB):
                                drained(pe, ("2", e, c, h), i)
                        for u in range(SUB):
                            ps, full = fill(pe, ("3", e, u), i)
                            for c in range(2):
                                m = mm(ps[:, 0:D], h2[:, c, u * P:(u + 1) * P], ew[2][:, e, c, :], start=(c == 0), stop=(c == 1))
                            m.then_inc(full, 1)

                    for h in range(HB):
                        ps, full = fill(pe, ("d", h), i)
                        mm(ps[:, :], fc1[:, :], hidden[:, 0, bass.ds(i * ROW + h * WIN, WIN)], start=True, stop=True).then_inc(full, 1)
                    pe.wait_ge(l_xT, i * 16 + 16)
                    for h in range(HB):
                        drained(pe, ("d", h), i)
                    for u in range(SUB):
                        ps, full = fill(pe, ("rec", u), i)
                        q = slice(u * P, (u + 1) * P)
                        mm(ps[:, 0:D], dT[:, q], fc2[:, :], start=True, stop=False)
                        mm(ps[:, 0:D], xT[:, 0, q], mix[:, 0, :], start=False, stop=False)
                        mm(ps[:, 0:D], xT[:, 1, q], mix[:, 1, :], start=False, stop=True).then_inc(full, 1)
                    for u in range(SUB):
                        pe.wait_ge(l_xln, i * SUB + (u + 1))
                        ps, full = fill(pe, ("turn", u), i)
                        nc.tensor.transpose(ps[:, 0:P], xl[:, u, 0:P], ident[:, :])
                        nc.tensor.transpose(ps[:, P:D], xl[:, u, P:D], ident[:, :]).then_inc(full, 1)
                    for u in range(SUB - SLIM, SUB):
                        drained(pe, ("turn", u), i)
                    for h in range(HB):
                        ps, full = fill(pe, ("r", h), i)
                        for c in range(2):
                            m = mm(ps[:, :], rw1[:, c, :], xlT[:, c, h * WIN:(h + 1) * WIN], start=(c == 0), stop=(c == 1))
                        m.then_inc(full, 1)
                    for h in range(HB):
                        drained(pe, ("r", h), i)
                    ps, full = fill(pe, ("logit", 0), i)
                    for u in range(SUB):
                        m = mm(ps[:, u * EXP:(u + 1) * EXP], rhT[:, u * P:(u + 1) * P], rw2[:, :], start=True, stop=True)
                    m.then_inc(full, 1)
                    dense("1", 0, ew[0], xlT)
                    dense("2", 0, ew[1], h1)
                    pe.wait_ge(l_rw, i + 1)
                    for g in range(2):
                        ps, full = fill(pe, ("rwT", g), i)
                        for u in range(4 * g, min(4 * g + 4, SUB)):
                            m = nc.tensor.transpose(ps[0:EXP, (u - 4 * g) * P:(u - 4 * g + 1) * P], rw[:, u, :], ident[:, :])
                        m.then_inc(full, 1)
                    for g in range(2):
                        drained(pe, ("rwT", g), i)
                    for u in range(SUB):
                        ps, full = fill(pe, ("b3", u), i)
                        mm(ps[:, 0:D], rwT[:, u * P:(u + 1) * P], eb3[:, :], start=True, stop=True).then_inc(full, 1)
                    for e in range(EXP):
                        if e + 1 < EXP:
                            dense("1", e + 1, ew[0], xlT)
                        last_layer(e)
                        if e + 1 < EXP:
                            dense("2", e + 1, ew[1], h1)


_INS = ["x", "src", "dst"] + [f"L0_gnn_{n}" for n in (
    "init_w1", "w1", "root_w1", "b1", "init_w2", "w2", "root_w2", "b2", "fc1_w", "fc1_b", "fc2_w", "fc2_b")] + [
    f"L0_mix_{n}" for n in ("wq", "wk", "wv", "wo", "bo", "ln_k_g", "ln_k_b", "ln_v_g", "ln_v_b")] + [
    f"L0_ffn_{n}" for n in ("router_w1", "router_b1", "router_w2", "router_b2", "expert_w1", "expert_b1",
                            "expert_w2", "expert_b2", "expert_w3", "expert_b3")]


def kernel(**inputs):
    import numpy as _np
    import concourse.bacc as _bacc
    from concourse import mybir as _mybir
    from concourse.bass_utils import run_bass_kernel_spmd as _run

    nc = _bacc.Bacc("TRN2", target_bir_lowering=False, num_devices=1)
    arrays, args = {}, {}
    for name in _INS:
        arr = _np.ascontiguousarray(inputs[name])
        arrays[f"in_{name}"] = arr
        args[name] = nc.dram_tensor(f"in_{name}", arr.shape, _mybir.dt.from_np(arr.dtype), kind="ExternalInput").ap()
    out = nc.dram_tensor("out_0", (N, D), F32, kind="ExternalOutput").ap()
    gps_layer(nc, args, out)
    r = _run(nc, [arrays], core_ids=[0])
    return r.results[0]["out_0"]
```
